# Optimizing a Trainium2 kernel written in Bass

```python
import numpy as np
import jax
import jax.numpy as jnp

def _softmax(x, axis=-1):
    return jax.nn.softmax(x, axis=axis)

def _gelu(x):
    return jax.nn.gelu(x, approximate=True)

def _silu(x):
    return jax.nn.silu(x)

def _sigmoid(x):
    return jax.nn.sigmoid(x)

def _layernorm(x, axis=-1, eps=1e-05):
    m = jnp.mean(x, axis=axis, keepdims=True)
    v = jnp.var(x, axis=axis, keepdims=True)
    return (x - m) / jnp.sqrt(v + eps)

def _scatter_add(tgt, idx, src, axis=0):
    return tgt.at[idx].add(src)

def _segment_sum(src, seg, n):
    return jax.ops.segment_sum(src, seg, n)
kernel_name = 'mk_lm_tower_d1_tok_ids512_r4_8cd2f6'

def setup_inputs(seed: int=0):
    np.random.seed(seed)
    _w = jnp.asarray

    def _rec_inputs():
        import jax
        import jax.numpy as jnp
        _rk = jax.random.key(seed)
        x = jax.random.randint(jax.random.fold_in(_rk, 1), (32, 256), 0, 1250, jnp.int32)
        return x
    x = _rec_inputs()

    def _L0_tok_setup():
        import jax, jax.numpy as jnp
        import numpy as np
        import math
        D_MODEL = 128
        MAX_LEN = 1250

        def _make_pe(max_len=MAX_LEN, d_model=D_MODEL):
            position = np.arange(max_len, dtype=np.float32)[:, None]
            div_term = np.exp(np.arange(0, d_model, 2, dtype=np.float32) * -(math.log(10000.0) / d_model))
            pe = np.zeros((max_len, d_model), dtype=np.float32)
            pe[:, 0::2] = np.sin(position * div_term)
            pe[:, 1::2] = np.cos(position * div_term)
            return jnp.asarray(pe)
        key = jax.random.key(seed)
        k1, _ = jax.random.split(key)
        delta_t = jax.random.randint(k1, (64, 1024), 0, MAX_LEN, dtype=jnp.int64 if jax.config.read('jax_enable_x64') else jnp.int32)
        pe = _make_pe()
        return {'delta_t': delta_t, 'pe': pe}
    _L0_tok_all = _L0_tok_setup()
    _L0_tok_in = {k: v for k, v in _L0_tok_all.items() if k in ('pe',)}
    del _L0_tok_all

    def _L0_attn_setup():
        import jax, jax.numpy as jnp
        import numpy as np
        B, S, D_IN = (8, 512, 128)
        H = 128
        GAMMA = 0.984375
        CHUNK = 2
        COUNTER = 1

        def _decay_matrix(s, gamma):
            i = jnp.arange(s)
            diff = i[:, None] - i[None, :]
            mask = diff >= 0
            Dm = jnp.where(mask, jnp.float32(gamma) ** jnp.where(mask, diff, 0).astype(jnp.float32), 0.0)
            Dm = Dm / jnp.sqrt(Dm.sum(-1))
            return Dm
        key = jax.random.key(seed)
        k1, k2 = jax.random.split(key, 2)
        x = jax.random.normal(k1, (B, S, D_IN), dtype=jnp.float32)
        W = jax.random.normal(k2, (D_IN, 3 * H), dtype=jnp.float32) * 0.02
        b = jnp.zeros((3 * H,), dtype=jnp.float32)
        return {'x': x, 'W': W, 'b': b}
    _L0_attn_all = _L0_attn_setup()
    _L0_attn_in = {k: v for k, v in _L0_attn_all.items() if k in ('W', 'b')}
    del _L0_attn_all

    def _L0_ffn_setup():
        import jax, jax.numpy as jnp
        import numpy as np
        K = 2
        key = jax.random.key(seed)
        ks = jax.random.split(key, 6)
        B, T, d, E, dff = (2, 512, 128, 8, 512)
        x = jax.random.normal(ks[0], (B, T, d), dtype=jnp.float32)
        Wg = jax.random.normal(ks[1], (d, E), dtype=jnp.float32) * 0.02
        W1 = jax.random.normal(ks[2], (E, d, dff), dtype=jnp.float32) * 0.02
        b1 = jnp.zeros((E, dff), dtype=jnp.float32)
        W2 = jax.random.normal(ks[3], (E, dff, d), dtype=jnp.float32) * 0.02
        b2 = jnp.zeros((E, d), dtype=jnp.float32)
        return {'x': x, 'Wg': Wg, 'W1': W1, 'b1': b1, 'W2': W2, 'b2': b2}
    _L0_ffn_all = _L0_ffn_setup()
    _L0_ffn_in = {k: v for k, v in _L0_ffn_all.items() if k in ('Wg', 'W1', 'b1', 'W2', 'b2')}
    del _L0_ffn_all
    return {'x': x, 'L0_tok_pe': _L0_tok_in['pe'], 'L0_attn_W': _L0_attn_in['W'], 'L0_attn_b': _L0_attn_in['b'], 'L0_ffn_Wg': _L0_ffn_in['Wg'], 'L0_ffn_W1': _L0_ffn_in['W1'], 'L0_ffn_b1': _L0_ffn_in['b1'], 'L0_ffn_W2': _L0_ffn_in['W2'], 'L0_ffn_b2': _L0_ffn_in['b2']}

def reference(x, L0_tok_pe, L0_attn_W, L0_attn_b, L0_ffn_Wg, L0_ffn_W1, L0_ffn_b1, L0_ffn_W2, L0_ffn_b2):
    import jax
    import jax.numpy as jnp

    def _L0_tok_ref(delta_t, pe):
        import jax, jax.numpy as jnp
        import numpy as np
        import math
        D_MODEL = 128
        MAX_LEN = 1250

        def _make_pe(max_len=MAX_LEN, d_model=D_MODEL):
            position = np.arange(max_len, dtype=np.float32)[:, None]
            div_term = np.exp(np.arange(0, d_model, 2, dtype=np.float32) * -(math.log(10000.0) / d_model))
            pe = np.zeros((max_len, d_model), dtype=np.float32)
            pe[:, 0::2] = np.sin(position * div_term)
            pe[:, 1::2] = np.cos(position * div_term)
            return jnp.asarray(pe)
        return pe[delta_t]

    def _L0_attn_ref(x, W, b):
        import jax, jax.numpy as jnp
        import numpy as np
        B, S, D_IN = (8, 512, 128)
        H = 128
        GAMMA = 0.984375
        CHUNK = 2
        COUNTER = 1

        def _decay_matrix(s, gamma):
            i = jnp.arange(s)
            diff = i[:, None] - i[None, :]
            mask = diff >= 0
            Dm = jnp.where(mask, jnp.float32(gamma) ** jnp.where(mask, diff, 0).astype(jnp.float32), 0.0)
            Dm = Dm / jnp.sqrt(Dm.sum(-1))
            return Dm
        Bv, s, d = x.shape
        h = W.shape[1] // 3
        Dm = _decay_matrix(s, GAMMA)
        Dsub = jax.lax.dynamic_slice(Dm, (COUNTER, COUNTER), (CHUNK, CHUNK))
        nc = s // CHUNK
        gc = jnp.float32(GAMMA) ** CHUNK
        gv = jnp.float32(GAMMA) ** (CHUNK - 1 - COUNTER)
        gq = jnp.float32(GAMMA) ** (COUNTER + 1)
        inv_sqrt_h = 1.0 / jnp.sqrt(jnp.float32(h))
        qkv = x @ W + b
        qkv = qkv.reshape(Bv, nc, CHUNK, 3 * h).transpose(1, 0, 2, 3)

        def step(state, qkv_t):
            q, k, v = jnp.split(qkv_t, 3, axis=-1)
            s_new = state * gc + jnp.einsum('bch,bcm->bhm', k, v * gv)
            att = jnp.einsum('bch,bdh->bcd', q, k) * inv_sqrt_h * Dsub
            denom = jnp.maximum(jnp.abs(att.sum(axis=1)), 1.0)
            att = att / denom[:, None, :]
            out = jnp.einsum('bcd,bdh->bch', att, v) + jnp.einsum('bch,bhm->bcm', q, state) * gq
            return (s_new, out)
        state0 = jnp.zeros((Bv, h, h), dtype=x.dtype)
        _, outs = jax.lax.scan(step, state0, qkv)
        return outs.transpose(1, 0, 2, 3).reshape(Bv, s, h)

    def _L0_ffn_ref(x, Wg, W1, b1, W2, b2):
        import jax, jax.numpy as jnp
        import numpy as np
        K = 2
        logits = jnp.einsum('btd,de->bte', x, Wg)
        probs = jax.nn.softmax(logits, axis=-1)
        top_p, _top_i = jax.lax.top_k(probs, K)
        top_p = top_p / jnp.sum(top_p, axis=-1, keepdims=True)
        b2_sum = jnp.sum(b2, axis=0)
        out = jnp.zeros_like(x)
        for i in range(K):
            w_in = x * top_p[..., i:i + 1]
            h = jax.nn.gelu(jnp.einsum('btd,edf->ebtf', w_in, W1) + b1[:, None, None, :], approximate=False)
            out = out + jnp.einsum('ebtf,efd->btd', h, W2) + b2_sum
        return out
    h = _L0_tok_ref(x, L0_tok_pe)
    h = h + _L0_attn_ref(_layernorm(h, axis=-1), L0_attn_W, L0_attn_b)
    h = h + _L0_ffn_ref(_layernorm(h, axis=-1), L0_ffn_Wg, L0_ffn_W1, L0_ffn_b1, L0_ffn_W2, L0_ffn_b2)
    return h

_drawn_inputs = setup_inputs


def setup_inputs(seed=0):
    import zlib

    import numpy as np

    out = dict(_drawn_inputs(seed))
    spreads = {'L0_attn_b': (0.0, 0.1), 'L0_ffn_b1': (0.0, 0.1), 'L0_ffn_b2': (0.0, 0.1)}
    factors = {}
    for name, (base, spread) in spreads.items():
        noise = np.random.default_rng([zlib.crc32(name.encode()), seed]).standard_normal(out[name].shape)
        drawn = base * np.exp(spread * noise) if base else spread * noise
        out[name] = jnp.asarray(drawn.astype(out[name].dtype))
    for name, factor in factors.items():
        out[name] = (out[name] * factor).astype(out[name].dtype)
    return out
```

```python
from contextlib import ExitStack

import numpy as np

import concourse.bass as bass
from concourse import mybir

F32 = mybir.dt.float32
F32R = mybir.dt.float32r
I32 = mybir.dt.int32
ALU = mybir.AluOpType
ACT = mybir.ActivationFunctionType
AX_X = mybir.AxisListType.X

P = 128
D = 128
SEQ = 256
BLK = 512
TILES = BLK // P
SEQS = BLK // SEQ
EXPERTS = 8
CHUNKS = 32
TOPK = 2
GAMMA = 0.984375
EPS = 1e-5

LAG = 6
ZBUFS = 4
SBUFS = 8
SCORE_W = 3 * P

POOL_AT = {"gather": (2, 4, 6, 8), "ids": 1, "rstd2": 10, "exp": 18, "rstd1": 19}
DVE_AT = {"v": 1, "att0": 3, "att1": 4, "att2": 5, "out": 8, "h_mid": 9, "stats2": 10, "moments2": 11, "norm2": 14,
          "x_lo": 17, "stats1": 18, "moments1": 19, "top": 20, "gate": 22, "norm1": 23}
ACT_AT = {"yT": 4, "x_hi": 15, "xaT": 24, "q": 27, "k": 28}
PE_AT = {"v": 1, "scores0": 3, "scores1": 4, "yT": 8, "attended": 10, "xT": 17, "logits": 20, "xaT": 26, "q": 28,
         "k": 29}

ROW_B1, ROW_BQKV, ROW_B2 = 0, CHUNKS, CHUNKS + 3
ROWS = ROW_B2 + EXPERTS


def attention_factors():
    chunk = np.arange(P) // 2
    gap = chunk[None, :] - chunk[:, None]
    diag = np.where(gap > 0, GAMMA ** (2.0 * np.maximum(gap, 0)), 0.0)
    off = GAMMA ** (2.0 * (gap + P // 2))
    between = np.concatenate([diag, off, diag], axis=1)
    norm = [np.sqrt(sum(GAMMA ** k for k in range(i + 1))) for i in range(3)]
    within = np.zeros((P, P))
    for s in range(P):
        for c in range(2):
            t = 2 * (s // 2) + c
            if t >= s:
                within[s, t] = GAMMA ** (t - s) / norm[1 + s % 2] / np.sqrt(float(D))
    return between.astype(np.float32), within.astype(np.float32)


def build(nc, tok, pe, w_qkv, b_qkv, w_gate, w1, b1, w2, b2, between_d, within_d, ident_d, out, gate_d):
    blocks = tok.shape[0] * tok.shape[1] // BLK
    tok_v = tok.rearrange("b (t p) -> p (b t)", p=P)
    out_v = out.rearrange("b (t p) d -> p (b t) d", p=P)

    ctx = ExitStack()
    with ctx:
        ctx.enter_context(nc.allow_non_contiguous_dma(reason="token ids and gate weights: 4-byte elements"))

        def sb(name, shape, dt=F32):
            return ctx.enter_context(nc.sbuf_tensor(name, shape, dt))

        def sem(name):
            return ctx.enter_context(nc.semaphore(name))

        w1_raw = sb("w1_raw", [P, CHUNKS, P])
        w1_hi = sb("w1_hi", [P, CHUNKS, P], F32R)
        w1_lo = sb("w1_lo", [P, CHUNKS, P], F32R)
        w2_sb = sb("w2_sb", [P, CHUNKS, D])
        wa = sb("wa", [P, 3 * D + EXPERTS])
        between = sb("between", [P, SCORE_W])
        within = sb("within", [P, P])
        ident = sb("ident", [P, P])
        rows = sb("rows", [ROWS, P])
        cols = sb("cols", [P, ROWS])
        b2_sum = sb("b2_sum", [P, 1])
        b2_twice = sb("b2_twice", [P, 1])
        bv = sb("bv", [P, D])
        minus_half = sb("minus_half", [P, TILES])
        warm = sb("warm", [P, TILES])
        eps = sb("eps", [P, TILES])
        euler = sb("euler", [P, TILES, TOPK])

        ids = sb("ids", [P, blocks * TILES], I32)
        ids_now = sb("ids_now", [P, TILES], I32)
        h_tok = sb("h_tok", [P, 2, TILES, D])
        stats = sb("stats", [P, TILES, 6])
        mean_var = sb("mean_var", [P, TILES, 2])
        var_eps = sb("var_eps", [P, TILES])
        rstd = sb("rstd", [P, TILES])
        xn = sb("xn", [P, TILES, D])
        xaT = sb("xaT", [P, BLK])
        qT = sb("qT", [P, BLK])
        kT = sb("kT", [P, BLK])
        v_sb = sb("v_sb", [P, TILES, D])
        att_in = sb("att_in", [P, TILES, P])
        att = sb("att", [P, SEQS, SCORE_W])
        att_sum = sb("att_sum", [P, TILES])
        att_abs = sb("att_abs", [P, TILES])
        att_den = sb("att_den", [P, TILES])
        att_rden = sb("att_rden", [P, TILES])
        h_mid = sb("h_mid", [P, 2, TILES, D])
        xT = sb("xT", [P, BLK])
        x_hi = sb("x_hi", [P, 2, BLK], F32R)
        x_lo = sb("x_lo", [P, 2, BLK], F32R)
        top = sb("top", [P, TILES, 8])
        top_rel = sb("top_rel", [P, TILES, TOPK])
        top_exp = sb("top_exp", [P, TILES, TOPK])
        top_sum = sb("top_sum", [P, TILES])
        top_rsum = sb("top_rsum", [P, TILES])
        gate = sb("gate", [P, TOPK, TILES])

        gate_all = sb("gate_all", [P, 2, TOPK, BLK])
        zs = sb("zs", [P, ZBUFS, TOPK, BLK])
        g = sb("g", [P, ZBUFS, TOPK, BLK])
        s = sb("s", [P, SBUFS, BLK])
        yT = sb("yT", [P, BLK])
        o = sb("o", [P, TILES, D])

        z = [ctx.enter_context(nc.psum_tensor(f"z{i}", [P, BLK], F32)) for i in range(ZBUFS)]
        acc = [ctx.enter_context(nc.psum_tensor(f"acc{i}", [P, BLK], F32)) for i in range(2)]
        even = ctx.enter_context(nc.psum_tensor("even", [P, BLK], F32))
        odd = ctx.enter_context(nc.psum_tensor("odd", [P, BLK], F32))

        wa_in, w1_in, w2_in, const_in, rows_in = (sem(n) for n in ("wa_in", "w1_in", "w2_in", "const_in", "rows_in"))
        w1_hi_ok, w1_lo_ok = sem("w1_hi_ok"), sem("w1_lo_ok")
        warmed = sem("warmed")
        cols_psum, cols_ok, b2_ok, b2_twice_ok, pool_consts = (
            sem(n) for n in ("cols_psum", "cols_ok", "b2_ok", "b2_twice_ok", "pool_consts"))
        first_ids_in, ids_in, ids_now_ok, rows_gathered = sem("first_ids_in"), sem("ids_in"), sem("ids_now_ok"), sem("rows_gathered")
        ln = [{n: sem(f"ln{w}_{n}") for n in ("stats", "moments", "var_eps", "rstd", "normed")} for w in (1, 2)]
        xaT_psum, xaT_ok = sem("xaT_psum"), sem("xaT_ok")
        q_psum, q_ok, k_psum, k_ok, v_psum, v_ok = (
            sem(n) for n in ("q_psum", "q_ok", "k_psum", "k_ok", "v_psum", "v_ok"))
        scores, att_in_ok, att_abs_ok, att_den_ok, att_rden_ok, att_between, att_ok = (
            sem(n) for n in ("scores", "att_in_ok", "att_abs_ok", "att_den_ok", "att_rden_ok", "att_between", "att_ok"))
        attended, h_mid_ok = sem("attended"), sem("h_mid_ok")
        xT_psum, xT_ok, x_hi_ok, x_lo_ok = sem("xT_psum"), sem("xT_ok"), sem("x_hi_ok"), sem("x_lo_ok")
        logits, top_ok, top_rel_ok, top_exp_ok, top_sum_ok, top_rsum_ok, gate_ok = (
            sem(n) for n in ("logits", "top_ok", "top_rel_ok", "top_exp_ok", "top_sum_ok", "top_rsum_ok", "gate_ok"))
        gate_out, gate_in = sem("gate_out"), sem("gate_in")
        z_ok, zs_ok, g_ok, s_ok = sem("z_ok"), sem("zs_ok"), sem("g_ok"), sem("s_ok")
        mixed, yT_ok, y_psum, o_ok, stored = (sem(n) for n in ("mixed", "yT_ok", "y_psum", "o_ok", "stored"))

        def run_blocks(body_of):
            eng, body = body_of
            body(0, 0)
            body(1, 1)
            with eng.Fori(1, blocks // 2 - 1) as j:
                body(j * 2, 0)
                body(j * 2 + 1, 1)
            body(blocks - 2, 0, rows_left=False)
            body(blocks - 1, 1, rows_left=False, front_left=False)

        def first(b, n=1):
            return isinstance(b, int) and b < n

        block = ctx.enter_context(nc.Block())

        @block.sync
        def _(sp):
            def spread_gate(a, par):
                sp.wait_ge(gate_ok, a + 1)
                sp.dma_start(gate_d[par].rearrange("k (t p) -> p k t", p=P), gate[:]).then_inc(gate_out, 16)
                sp.wait_ge(gate_out, a * 16 + 16)
                if not first(a, 2):
                    sp.wait_ge(zs_ok, a * CHUNKS - CHUNKS)
                sp.dma_start(gate_all[:, par], gate_d[par:par + 1].broadcast_to([P, TOPK, BLK])).then_inc(gate_in, 16)

            def store(b):
                sp.wait_ge(o_ok, b + 1)
                sp.dma_start(out_v[:, bass.ds(b * TILES, TILES), :], o[:]).then_inc(stored, 16)

            sp.dma_start(ids[:, 0:TILES], tok_v[:, 0:TILES]).then_inc(first_ids_in, 16)
            sp.dma_start(ident[:], ident_d).then_inc(const_in, 16)
            sp.dma_start(wa[:, 0:3 * D], w_qkv).then_inc(wa_in, 16)
            sp.dma_start(wa[:, 3 * D:], w_gate).then_inc(wa_in, 16)
            sp.dma_start(rows[ROW_BQKV:ROW_B2, :], b_qkv.rearrange("(r d) -> r d", d=P)).then_inc(rows_in, 16)
            sp.dma_start(rows[ROW_B1:ROW_BQKV, :], b1.rearrange("e (c f) -> (e c) f", f=P)).then_inc(rows_in, 16)
            sp.dma_start(rows[ROW_B2:ROWS, :], b2).then_inc(rows_in, 16)
            sp.dma_start(bv[:], b_qkv[2 * D:3 * D].rearrange("(o d) -> o d", o=1).broadcast_to([P, D])
                         ).then_inc(const_in, 16)
            sp.dma_start(between[:], between_d).then_inc(const_in, 16)
            sp.dma_start(within[:], within_d).then_inc(const_in, 16)
            sp.wait_ge(rows_gathered, 16 * TILES)
            sp.dma_start(w1_raw[:].rearrange("p (e c) f -> p e (c f)", e=EXPERTS),
                         w1.rearrange("e d f -> d e f")).then_inc(w1_in, 16)
            sp.dma_start(ids[:, TILES:], tok_v[:, TILES:]).then_inc(ids_in, 16)
            sp.dma_start(w2_sb[:], w2.rearrange("e (c f) d -> f (e c) d", f=P)).then_inc(w2_in, 16)
            spread_gate(0, 0)

            def body(b, par, rows_left=True, front_left=True):
                if not first(b):
                    store(b - 1)
                if front_left:
                    spread_gate(b + 1, 1 - par)

            run_blocks((sp, body))
            store(blocks - 1)
            sp.wait_ge(stored, 16 * blocks)

        @block.gpsimd
        def _(pool):
            def take_ids(a):
                if not first(a, 2):
                    pool.wait_ge(rows_gathered, a * (16 * TILES))
                pool.tensor_copy(ids_now[:], ids[:, bass.ds(a * TILES, TILES)]).then_inc(ids_now_ok, 1)

            def await_ids(a):
                pool.wait_ge(ids_now_ok, a + 1)
                if not first(a, 2):
                    pool.wait_ge(h_mid_ok, a - 1)

            def gather(a, par, t):
                pool.indirect_dma_start(out=h_tok[:, par, t, :], out_offset=None, in_=pe,
                                        in_offset=bass.IndirectOffsetOnAxis(ap=ids_now[:, t:t + 1], axis=0)
                                        ).then_inc(rows_gathered, 16)

            def rstd_of(w, a):
                pool.wait_ge(ln[w]["moments"], a * TILES + TILES)
                pool.tensor_tensor(var_eps[:], mean_var[:, :, 1], eps[:], ALU.add).then_inc(ln[w]["var_eps"], 1)
                pool.wait_ge(ln[w]["var_eps"], a + 1)
                pool.tensor_tensor(rstd[:], var_eps[:], minus_half[:], ALU.pow).then_inc(ln[w]["rstd"], 1)

            def exps(a):
                pool.wait_ge(top_rel_ok, a + 1)
                pool.tensor_tensor(top_exp[:], euler[:], top_rel[:], ALU.pow).then_inc(top_exp_ok, 1)

            def add(b, c):
                pool.wait_ge(g_ok, b * CHUNKS + (c + 1))
                if not (first(b) and c < SBUFS):
                    pool.wait_ge(mixed, b * CHUNKS + (c - SBUFS + 1))
                pool.tensor_tensor(s[:, c % SBUFS, :], g[:, c % ZBUFS, 0, :], g[:, c % ZBUFS, 1, :],
                                   ALU.add).then_inc(s_ok, 1)

            pool.memset(minus_half[:], -0.5).then_inc(pool_consts, 1)
            pool.memset(eps[:], EPS).then_inc(pool_consts, 1)
            pool.memset(euler[:], float(np.e)).then_inc(pool_consts, 1)
            pool.wait_ge(first_ids_in, 16)
            take_ids(0)
            await_ids(0)
            for t in range(TILES):
                gather(0, 0, t)
            rstd_of(0, 0)
            pool.wait_ge(ids_in, 16)
            pool.wait_ge(rows_gathered, 16 * TILES)
            take_ids(1)
            await_ids(1)
            for t in range(TILES):
                gather(1, 1, t)
            rstd_of(1, 0)
            rstd_of(0, 1)
            exps(0)

            def body(b, par, rows_left=True, front_left=True):
                for c in range(CHUNKS):
                    if rows_left and c == POOL_AT["gather"][0]:
                        await_ids(b + 2)
                    add(b, c)
                    if rows_left and c == POOL_AT["ids"]:
                        take_ids(b + 2)
                    if rows_left and c == POOL_AT["rstd1"]:
                        rstd_of(0, b + 2)
                    if rows_left and c in POOL_AT["gather"]:
                        gather(b + 2, par, POOL_AT["gather"].index(c))
                    if front_left and c == POOL_AT["rstd2"]:
                        rstd_of(1, b + 1)
                    if front_left and c == POOL_AT["exp"]:
                        exps(b + 1)

            run_blocks((pool, body))

        @block.scalar
        def _(act):
            b1_col, b_col = cols[:, ROW_B1:ROW_BQKV], cols[:, ROW_BQKV:ROW_B2]

            def round_off(dst, src, done):
                act.activation(dst, src, ACT.Copy).then_inc(done, 1)

            def xa_copy(a):
                act.wait_ge(xaT_psum, a + 1)
                act.activation(xaT[:], odd[:], ACT.Copy).then_inc(xaT_ok, 1)

            def project(a, psum, psum_ok, dst, ok, bias):
                act.wait_ge(psum_ok, a + 1)
                act.activation(dst[:], psum[:], ACT.Identity, bias=bias).then_inc(ok, 1)

            def x_high(a, par):
                act.wait_ge(xT_psum, a + 1)
                round_off(x_hi[:, par, :], odd[:], x_hi_ok)
                act.activation(xT[:], odd[:], ACT.Copy).then_inc(xT_ok, 1)

            def y_bias(b, par):
                act.wait_ge(mixed, b * CHUNKS + CHUNKS)
                if not first(b):
                    act.wait_ge(y_psum, b)
                act.activation(yT[:], acc[par][:], ACT.Identity, bias=b2_twice[:, 0:1]).then_inc(yT_ok, 1)

            def gelus(b, c):
                act.wait_ge(zs_ok, b * CHUNKS + (c + 1))
                if not (first(b) and c < ZBUFS):
                    act.wait_ge(s_ok, b * CHUNKS + (c - ZBUFS + 1))
                act.activation(g[:, c % ZBUFS], zs[:, c % ZBUFS], ACT.Gelu,
                               bias=b1_col[:, c:c + 1]).then_inc(g_ok, 1)

            act.wait_ge(pool_consts, 3)
            act.activation(warm[:], eps[:], ACT.Gelu).then_inc(warmed, 1)
            act.wait_ge(cols_psum, 1)
            act.activation(cols[:], even[:, 0:ROWS], ACT.Copy).then_inc(cols_ok, 1)
            act.wait_ge(cols_ok, 1)
            xa_copy(0)
            act.wait_ge(w1_in, 16)
            for e in range(EXPERTS):
                part = slice(e * CHUNKS // EXPERTS, (e + 1) * CHUNKS // EXPERTS)
                round_off(w1_hi[:, part], w1_raw[:, part], w1_hi_ok)
                if e == 0:
                    project(0, even, q_psum, qT, q_ok, b_col[:, 0:1])
                    project(0, odd, k_psum, kT, k_ok, b_col[:, 1:2])
            x_high(0, 0)
            xa_copy(1)
            project(1, even, q_psum, qT, q_ok, b_col[:, 0:1])
            project(1, odd, k_psum, kT, k_ok, b_col[:, 1:2])
            act.wait_ge(b2_twice_ok, 1)

            def body(b, par, rows_left=True, front_left=True):
                for c in range(CHUNKS):
                    gelus(b, c)
                    if c == ACT_AT["yT"] and not first(b):
                        y_bias(b - 1, 1 - par)
                    if front_left and c == ACT_AT["x_hi"]:
                        x_high(b + 1, 1 - par)
                    if rows_left and c == ACT_AT["xaT"]:
                        xa_copy(b + 2)
                    if rows_left and c == ACT_AT["q"]:
                        project(b + 2, even, q_psum, qT, q_ok, b_col[:, 0:1])
                    if rows_left and c == ACT_AT["k"]:
                        project(b + 2, odd, k_psum, kT, k_ok, b_col[:, 1:2])

            run_blocks((act, body))
            y_bias(blocks - 1, 1)

        @block.vector
        def _(dve):
            def statistics(w, a, src, ready, count):
                dve.wait_ge(ready, count)
                for t in range(TILES):
                    dve.bn_stats(stats[:, t, :], src[:, t, :]).then_inc(ln[w]["stats"], 1)

            def await_statistics(w, a):
                dve.wait_ge(ln[w]["stats"], a * TILES + TILES)

            def moments(w, a):
                for t in range(TILES):
                    dve.bn_aggr(mean_var[:, t, :], stats[:, t, :]).then_inc(ln[w]["moments"], 1)

            def normalise(w, a, src):
                dve.wait_ge(ln[w]["rstd"], a + 1)
                for t in range(TILES):
                    dve.tensor_scalar(xn[:, t, :], src[:, t, :], mean_var[:, t, 0:1], rstd[:, t:t + 1],
                                      ALU.subtract, ALU.mult).then_inc(ln[w]["normed"], 1)

            def low(dst, psum, hi, hi_ok, count, done):
                dve.wait_ge(hi_ok, count)
                dve.tensor_tensor(dst, psum, hi.bitcast(F32), ALU.subtract).then_inc(done, 1)

            def v_bias(a):
                dve.wait_ge(v_psum, a + 1)
                dve.tensor_tensor(v_sb[:], even[:].rearrange("p (t d) -> p t d", t=TILES),
                                  bv[:].rearrange("p (o d) -> p o d", o=1).broadcast_to([P, TILES, D]), ALU.add
                                  ).then_inc(v_ok, 1)

            def diagonal(n):
                at = (n % 2) * 2 * P
                return slice(at, at + P)

            def att_seq(a, r):
                bank = (odd, even)[r]
                dve.wait_ge(scores, a * SEQS + (r + 1))
                for n in (2 * r, 2 * r + 1):
                    dve.tensor_tensor_reduce(att_in[:, n, :], bank[:, diagonal(n)], within[:], 1.0, 0.0,
                                             ALU.mult, ALU.add, att_sum[:, n:n + 1]).then_inc(att_in_ok, 1)
                dve.tensor_tensor(att[:, r, :], bank[:, 0:SCORE_W], between[:], ALU.mult).then_inc(att_between, 1)

            def att_norm(a):
                dve.wait_ge(att_in_ok, a * TILES + TILES)
                dve.scalar_tensor_tensor(out=att_abs[:], in0=att_sum[:], scalar=-1.0, in1=att_sum[:],
                                         op0=ALU.mult, op1=ALU.max).then_inc(att_abs_ok, 1)
                dve.wait_ge(att_abs_ok, a + 1)
                dve.tensor_scalar(att_den[:], att_abs[:], 1.0, None, ALU.max).then_inc(att_den_ok, 1)
                dve.wait_ge(att_den_ok, a + 1)
                dve.reciprocal(att_rden[:], att_den[:]).then_inc(att_rden_ok, 1)
                dve.wait_ge(att_rden_ok, a + 1)
                for n in range(TILES):
                    here = att[:, n // 2, diagonal(n)]
                    dve.wait_ge(att_between, a * SEQS + (n // 2 + 1))
                    dve.scalar_tensor_tensor(out=here, in0=att_in[:, n, :], scalar=att_rden[:, n:n + 1], in1=here,
                                             op0=ALU.mult, op1=ALU.add).then_inc(att_ok, 1)

            def residual(a, par):
                dve.wait_ge(attended, a + 1)
                if not first(a, 2):
                    dve.wait_ge(o_ok, a - 1)
                dve.tensor_tensor(h_mid[:, par], even[:].rearrange("p (t d) -> p t d", t=TILES), h_tok[:, par],
                                  ALU.add).then_inc(h_mid_ok, 1)

            def await_logits(a):
                dve.wait_ge(logits, a + 1)

            def top_two(a):
                for t in range(TILES):
                    dve.max(top[:, t, :], even[:, t * EXPERTS:(t + 1) * EXPERTS]).then_inc(top_ok, 1)
                dve.wait_ge(top_ok, a * TILES + TILES)
                dve.tensor_tensor(top_rel[:], top[:, :, 0:TOPK], top[:, :, 0:1].broadcast_to([P, TILES, TOPK]),
                                  ALU.subtract).then_inc(top_rel_ok, 1)

            def gates(a):
                dve.wait_ge(top_exp_ok, a + 1)
                dve.tensor_tensor(top_sum[:], top_exp[:, :, 0], top_exp[:, :, 1], ALU.add).then_inc(top_sum_ok, 1)
                dve.wait_ge(top_sum_ok, a + 1)
                dve.reciprocal(top_rsum[:], top_sum[:]).then_inc(top_rsum_ok, 1)
                dve.wait_ge(top_rsum_ok, a + 1)
                if not first(a):
                    dve.wait_ge(gate_out, a * 16)
                dve.tensor_tensor(gate[:], top_exp[:].rearrange("p t k -> p k t"),
                                  top_rsum[:].rearrange("p (o t) -> p o t", o=1).broadcast_to([P, TOPK, TILES]),
                                  ALU.mult).then_inc(gate_ok, 1)

            def finish(b, par):
                dve.wait_ge(y_psum, b + 1)
                if not first(b):
                    dve.wait_ge(stored, b * 16)
                dve.tensor_tensor(o[:], odd[:].rearrange("p (t d) -> p t d", t=TILES), h_mid[:, par],
                                  ALU.add).then_inc(o_ok, 1)

            def scale(b, par, c):
                if c == 0:
                    dve.wait_ge(gate_in, b * 16 + 16)
                dve.wait_ge(z_ok, b * CHUNKS + (c + 1))
                if not (first(b) and c < ZBUFS):
                    dve.wait_ge(g_ok, b * CHUNKS + (c - ZBUFS + 1))
                both = z[c % ZBUFS][:].rearrange("p (o n) -> p o n", o=1).broadcast_to([P, TOPK, BLK])
                dve.tensor_tensor(zs[:, c % ZBUFS], both, gate_all[:, par], ALU.mult).then_inc(zs_ok, 1)

            statistics(0, 0, h_tok[:, 0], rows_gathered, 16 * TILES)
            await_statistics(0, 0)
            moments(0, 0)
            normalise(0, 0, h_tok[:, 0])
            dve.wait_ge(cols_ok, 1)
            dve.reduce_sum(b2_sum[:], cols[:, ROW_B2:ROWS], AX_X).then_inc(b2_ok, 1)
            dve.wait_ge(b2_ok, 1)
            dve.tensor_scalar(b2_twice[:], b2_sum[:], float(TOPK), None, ALU.mult).then_inc(b2_twice_ok, 1)
            dve.wait_ge(const_in, 64)

            def w1_low(e):
                part = slice(e * CHUNKS // EXPERTS, (e + 1) * CHUNKS // EXPERTS)
                low(w1_lo[:, part], w1_raw[:, part], w1_hi[:, part], w1_hi_ok, e + 1, w1_lo_ok)

            for e in range(EXPERTS):
                w1_low(e)
            v_bias(0)
            att_seq(0, 0)
            att_seq(0, 1)
            att_norm(0)
            residual(0, 0)
            statistics(1, 0, h_mid[:, 0], h_mid_ok, 1)
            await_statistics(1, 0)
            moments(1, 0)
            normalise(1, 0, h_mid[:, 0])
            statistics(0, 1, h_tok[:, 1], rows_gathered, 2 * 16 * TILES)
            await_statistics(0, 1)
            moments(0, 1)
            low(x_lo[:, 0], odd[:], x_hi[:, 0], xT_ok, 1, x_lo_ok)
            normalise(0, 1, h_tok[:, 1])
            await_logits(0)
            top_two(0)
            gates(0)

            def body(b, par, rows_left=True, front_left=True):
                a, nxt = b + 1, 1 - par
                for c in range(CHUNKS):
                    if front_left and c == DVE_AT["moments2"]:
                        await_statistics(1, a)
                    if rows_left and c == DVE_AT["moments1"]:
                        await_statistics(0, b + 2)
                    if front_left and c == DVE_AT["top"]:
                        await_logits(a)
                    scale(b, par, c)
                    if c == DVE_AT["out"] and not first(b):
                        finish(b - 1, nxt)
                    if front_left and c == DVE_AT["v"]:
                        v_bias(a)
                    if front_left and c == DVE_AT["att0"]:
                        att_seq(a, 0)
                    if front_left and c == DVE_AT["att1"]:
                        att_seq(a, 1)
                    if front_left and c == DVE_AT["att2"]:
                        att_norm(a)
                    if front_left and c == DVE_AT["h_mid"]:
                        residual(a, nxt)
                    if front_left and c == DVE_AT["stats2"]:
                        statistics(1, a, h_mid[:, nxt], h_mid_ok, a + 1)
                    if front_left and c == DVE_AT["moments2"]:
                        moments(1, a)
                    if front_left and c == DVE_AT["norm2"]:
                        normalise(1, a, h_mid[:, nxt])
                    if front_left and c == DVE_AT["x_lo"]:
                        low(x_lo[:, nxt], odd[:], x_hi[:, nxt], xT_ok, a + 1, x_lo_ok)
                    if front_left and c == DVE_AT["top"]:
                        top_two(a)
                    if front_left and c == DVE_AT["gate"]:
                        gates(a)
                    if rows_left and c == DVE_AT["stats1"]:
                        statistics(0, b + 2, h_tok[:, par], rows_gathered, b * (16 * TILES) + 3 * 16 * TILES)
                    if rows_left and c == DVE_AT["moments1"]:
                        moments(0, b + 2)
                    if rows_left and c == DVE_AT["norm1"]:
                        normalise(0, b + 2, h_tok[:, par])

            run_blocks((dve, body))
            finish(blocks - 1, 1)

        @block.tensor
        def _(te):
            def passes(psum, w_hi, w_lo, m_hi, m_lo):
                te.matmul(psum, w_hi, m_hi, start=True, stop=False)
                te.matmul(psum, w_hi, m_lo, start=False, stop=False)
                return te.matmul(psum, w_lo, m_hi, start=False, stop=True)

            def turn(normed, bank, done):
                te.wait_ge(*normed)
                for t in range(TILES):
                    tr = te.transpose(bank[:, t * P:(t + 1) * P], xn[:, t, :], ident[:])
                tr.then_inc(done, 1)

            def xa_turn(a):
                if not first(a):
                    te.wait_ge(x_lo_ok, a)
                turn((ln[0]["normed"], a * TILES + TILES), odd, xaT_psum)

            def query(a):
                te.wait_ge(xaT_ok, a + 1)
                if not first(a):
                    te.wait_ge(top_rel_ok, a)
                te.matmul(even[:], wa[:, 0:D], xaT[:], start=True, stop=True).then_inc(q_psum, 1)

            def key(a):
                te.matmul(odd[:], wa[:, D:2 * D], xaT[:], start=True, stop=True).then_inc(k_psum, 1)

            def value(a):
                te.wait_ge(q_ok, a + 1)
                for t in range(TILES):
                    tok_t = slice(t * P, (t + 1) * P)
                    mm = te.matmul(even[:, tok_t], xaT[:, tok_t], wa[:, 2 * D:3 * D], start=True, stop=True)
                mm.then_inc(v_psum, 1)

            def score(a, r):
                if r == 0:
                    te.wait_ge(k_ok, a + 1)
                else:
                    te.wait_ge(v_ok, a + 1)
                bank, at = (odd, even)[r], r * SEQ
                te.matmul(bank[:, 0:2 * P], kT[:, at:at + P], qT[:, at:at + 2 * P], start=True, stop=True)
                te.matmul(bank[:, 2 * P:3 * P], kT[:, at + P:at + 2 * P], qT[:, at + P:at + 2 * P],
                          start=True, stop=True).then_inc(scores, 1)

            def y_turn(b, bank_read, count):
                te.wait_ge(bank_read, count)
                te.wait_ge(yT_ok, b + 1)
                for t in range(TILES):
                    tr = te.transpose(odd[:, t * P:(t + 1) * P], yT[:, t * P:(t + 1) * P], ident[:])
                tr.then_inc(y_psum, 1)

            def attend(a):
                te.wait_ge(att_ok, a * TILES + TILES)
                for r in range(SEQS):
                    at, t0 = r * SEQ, 2 * r
                    te.matmul(even[:, at:at + P], att[:, r, 0:P], v_sb[:, t0, :], start=True, stop=True)
                    te.matmul(even[:, at + P:at + 2 * P], att[:, r, P:2 * P], v_sb[:, t0, :], start=True, stop=False)
                    mm = te.matmul(even[:, at + P:at + 2 * P], att[:, r, 2 * P:3 * P], v_sb[:, t0 + 1, :],
                                   start=False, stop=True)
                mm.then_inc(attended, 1)

            def x_turn(a):
                if not first(a, 2):
                    te.wait_ge(o_ok, a - 1)
                turn((ln[1]["normed"], a * TILES + TILES), odd, xT_psum)

            def logit(a):
                te.wait_ge(xT_ok, a + 1)
                te.wait_ge(h_mid_ok, a + 1)
                for t in range(TILES):
                    tok_t = slice(t * P, (t + 1) * P)
                    mm = te.matmul(even[:, t * EXPERTS:(t + 1) * EXPERTS], xT[:, tok_t], wa[:, 3 * D:],
                                   start=True, stop=True)
                mm.then_inc(logits, 1)

            def hidden(b, par, c):
                if not (first(b) and c < ZBUFS):
                    te.wait_ge(zs_ok, b * CHUNKS + (c - ZBUFS + 1))
                passes(z[c % ZBUFS][:], w1_hi[:, c, :], w1_lo[:, c, :], x_hi[:, par], x_lo[:, par]).then_inc(z_ok, 1)

            def mix(b, par, c):
                te.wait_ge(s_ok, b * CHUNKS + (c + 1))
                if c == 0 and not first(b, 2):
                    te.wait_ge(yT_ok, b - 1)
                te.matmul(acc[par][:], w2_sb[:, c, :], s[:, c % SBUFS, :], start=c == 0, stop=c == CHUNKS - 1
                          ).then_inc(mixed, 1)

            te.wait_ge(const_in, 64)
            te.wait_ge(rows_in, 48)
            te.transpose(even[:, 0:ROWS], rows[:], ident[0:ROWS, 0:ROWS]).then_inc(cols_psum, 1)
            xa_turn(0)
            te.wait_ge(wa_in, 32)
            te.wait_ge(cols_ok, 1)
            query(0)
            key(0)
            value(0)
            score(0, 0)
            score(0, 1)
            attend(0)
            x_turn(0)
            logit(0)
            xa_turn(1)
            query(1)
            key(1)
            te.wait_ge(w1_lo_ok, EXPERTS)
            te.wait_ge(w2_in, 16)

            def body(b, par, rows_left=True, front_left=True):
                a, nxt = b + 1, 1 - par
                for c in range(CHUNKS):
                    if c == 0:
                        te.wait_ge(x_lo_ok, b + 1)
                    hidden(b, par, c)
                    if c >= LAG:
                        mix(b, par, c - LAG)
                    elif not first(b):
                        mix(b - 1, nxt, CHUNKS + c - LAG)
                    if c == PE_AT["yT"] and not first(b):
                        if front_left:
                            y_turn(b - 1, att_between, a * SEQS + 1)
                        else:
                            y_turn(b - 1, x_lo_ok, b + 1)
                    if front_left and c == PE_AT["v"]:
                        value(a)
                    if front_left and c == PE_AT["scores0"]:
                        score(a, 0)
                    if front_left and c == PE_AT["scores1"]:
                        score(a, 1)
                    if front_left and c == PE_AT["attended"]:
                        attend(a)
                    if front_left and c == PE_AT["xT"]:
                        x_turn(a)
                    if front_left and c == PE_AT["logits"]:
                        logit(a)
                    if rows_left and c == PE_AT["xaT"]:
                        xa_turn(a + 1)
                    if rows_left and c == PE_AT["q"]:
                        query(a + 1)
                    if rows_left and c == PE_AT["k"]:
                        key(a + 1)

            run_blocks((te, body))
            for c in range(CHUNKS - LAG, CHUNKS):
                mix(blocks - 1, 1, c)
            y_turn(blocks - 1, o_ok, blocks - 1)


_INS = ["x", "L0_tok_pe", "L0_attn_W", "L0_attn_b", "L0_ffn_Wg", "L0_ffn_W1", "L0_ffn_b1", "L0_ffn_W2", "L0_ffn_b2"]


def kernel(**inputs):
    import concourse.bacc as bacc
    from concourse.bass_utils import run_bass_kernel_spmd

    nc = bacc.Bacc("TRN2", target_bir_lowering=False, num_devices=1)
    arrays = {f"in_{n}": np.ascontiguousarray(inputs[n]) for n in _INS}
    between, within = attention_factors()
    arrays.update(const_between=between, const_within=within, const_ident=np.eye(P, dtype=np.float32))
    args = [nc.dram_tensor(n, a.shape, mybir.dt.from_np(a.dtype), kind="ExternalInput").ap() for n, a in arrays.items()]
    shape = (*inputs["x"].shape, D)
    out = nc.dram_tensor("out_h", shape, F32, kind="ExternalOutput").ap()
    gate_d = nc.dram_tensor("gate_by_token", (2, TOPK, BLK), F32, kind="Internal").ap()
    build(nc, *args, out, gate_d)
    r = run_bass_kernel_spmd(nc, [arrays], core_ids=[0])
    return r.results[0]["out_h"]
```

```python
from contextlib import ExitStack

import numpy as np

import concourse.bass as bass
from concourse import mybir

F32 = mybir.dt.float32
F32R = mybir.dt.float32r
I32 = mybir.dt.int32
ALU = mybir.AluOpType
ACT = mybir.ActivationFunctionType
AX_X = mybir.AxisListType.X

P = 128
D = 128
SEQ = 256
BLK = 512
TILES = BLK // P
SEQS = BLK // SEQ
EXPERTS = 8
CHUNKS = 32
TOPK = 2
GAMMA = 0.984375
EPS = 1e-5

LAG = 8
ZBUFS = 4
SBUFS = 8
SPLIT_CHUNKS = range(0, CHUNKS, 4)
SPLIT_BUFS = 2
HI_LAG, LO_LAG = 2, 4
SCORE_W = 3 * P

POOL_AT = {"ids": 1, "gather": (3, 9, 15, 25), "rstd": 12, "exp": 20}
DVE_AT = {"att0": 5, "att1": 6, "att2": 7, "out": 10, "h_mid": 11, "stats": 12, "moments": 13, "shift": 15,
          "x_lo": 19, "top": 21, "gate": 24}
ACT_AT = {"q": 0, "k": 1, "yT": 7, "norm": 14, "x_hi": 17}
PE_AT = {"q": 1, "k": 2, "scores0": 5, "scores1": 6, "yT": 10, "attended": 11, "xT": 19, "logits": 22}

COLS_H, COLS_Q, COLS_K, COLS_V = (slice(n * D, (n + 1) * D) for n in range(4))
TAB_W = 4 * D
TAB_HALVES = (slice(0, 5), slice(5, 10))
TAB_BANKS = 3
TAB_EARLY = 4
WARM_UPS, WARM_UPS_AGAIN = 12, 8
TAB_STORE = 2

ROW_B1, ROW_B2 = 0, CHUNKS
ROW_BQ = ROW_B2 + EXPERTS
ROW_BK = ROW_BQ + 1
ROWS = ROW_BK + 1


def attention_factors():
    chunk = np.arange(P) // 2
    gap = chunk[None, :] - chunk[:, None]
    diag = np.where(gap > 0, GAMMA ** (2.0 * np.maximum(gap, 0)), 0.0)
    off = GAMMA ** (2.0 * (gap + P // 2))
    between = np.concatenate([diag, off, diag], axis=1)
    norm = [np.sqrt(sum(GAMMA ** k for k in range(i + 1))) for i in range(3)]
    within = np.zeros((P, P))
    for s in range(P):
        for c in range(2):
            t = 2 * (s // 2) + c
            if t >= s:
                within[s, t] = GAMMA ** (t - s) / norm[1 + s % 2] / np.sqrt(float(D))
    return between.astype(np.float32), within.astype(np.float32)


def build(nc, tok, pe, w_qkv, b_qkv, w_gate, w1, b1, w2, b2, between_d, within_d, ident_d, out, table_d, gate_d):
    blocks = tok.shape[0] * tok.shape[1] // BLK
    tok_v = tok.rearrange("b (t p) -> p (b t)", p=P)
    ids_all = pe.shape[0]
    tab_tiles = -(-ids_all // P)
    tab_p = ids_all // tab_tiles
    assert tab_p * tab_tiles == ids_all
    out_v = out.rearrange("b (t p) d -> p (b t) d", p=P)

    ctx = ExitStack()
    with ctx:
        ctx.enter_context(nc.allow_non_contiguous_dma(reason="token ids and gate weights: 4-byte elements"))

        def sb(name, shape, dt=F32):
            return ctx.enter_context(nc.sbuf_tensor(name, shape, dt))

        def sem(name):
            return ctx.enter_context(nc.semaphore(name))

        w1_raw = sb("w1_raw", [P, CHUNKS, P])
        w1_hi = sb("w1_hi", [P, CHUNKS, P], F32R)
        w1_lo = sb("w1_lo", [P, CHUNKS, P], F32R)
        w2_sb = sb("w2_sb", [P, CHUNKS, D])
        w2_hi = sb("w2_hi", [P, len(SPLIT_CHUNKS), D], F32R)
        w2_lo = sb("w2_lo", [P, len(SPLIT_CHUNKS), D], F32R)
        wa = sb("wa", [P, 3 * D + EXPERTS])
        between = sb("between", [P, SCORE_W])
        within = sb("within", [P, P])
        ident = sb("ident", [P, P])
        small = sb("small", [ROWS, P])
        cols = sb("cols", [P, ROWS])
        b2_sum = sb("b2_sum", [P, 1])
        b2_twice = sb("b2_twice", [P, 1])
        b_all = sb("b_all", [P, 3 * D])
        minus_half = sb("minus_half", [P, tab_tiles])
        warm = sb("warm", [P, TILES])
        eps = sb("eps", [P, tab_tiles])
        euler = sb("euler", [P, TILES, TOPK])

        tab_room = sb("tab_room", [P, tab_tiles * TAB_W])
        tab = tab_room[0:tab_p].rearrange("p (j n) -> p j n", j=tab_tiles)
        tab_stats = sb("tab_stats", [tab_p, tab_tiles, 6])
        tab_mean_var = sb("tab_mean_var", [tab_p, tab_tiles, 2])
        tab_var_eps = sb("tab_var_eps", [tab_p, tab_tiles])
        tab_rstd = sb("tab_rstd", [tab_p, tab_tiles])
        tab_xn = sb("tab_xn", [tab_p, tab_tiles, D])
        tab_xnT = sb("tab_xnT", [P, tab_tiles, tab_p])

        ids = sb("ids", [P, blocks * TILES], I32)
        ids_now = sb("ids_now", [P, TILES], I32)
        rows = sb("rows", [P, 2, TILES, TAB_W])
        stats = sb("stats", [P, TILES, 6])
        mean_var = sb("mean_var", [P, TILES, 2])
        var_eps = sb("var_eps", [P, TILES])
        rstd = sb("rstd", [P, TILES])
        minus_shift = sb("minus_shift", [P, TILES])
        xn = sb("xn", [P, TILES, D])
        qT = sb("qT", [P, BLK])
        kT = sb("kT", [P, BLK])
        att_in = sb("att_in", [P, TILES, P])
        att = sb("att", [P, SEQS, SCORE_W])
        att_sum = sb("att_sum", [P, TILES])
        att_abs = sb("att_abs", [P, TILES])
        att_den = sb("att_den", [P, TILES])
        att_rden = sb("att_rden", [P, TILES])
        h_mid = sb("h_mid", [P, 2, TILES, D])
        xT = sb("xT", [P, BLK])
        x_hi = sb("x_hi", [P, 2, BLK], F32R)
        x_lo = sb("x_lo", [P, 2, BLK], F32R)
        top = sb("top", [P, TILES, 8])
        top_rel = sb("top_rel", [P, TILES, TOPK])
        top_exp = sb("top_exp", [P, TILES, TOPK])
        top_sum = sb("top_sum", [P, TILES])
        top_rsum = sb("top_rsum", [P, TILES])
        gate = sb("gate", [P, TOPK, TILES])

        spare = w1_raw[:].rearrange("p c f -> p (c f)").rearrange("p (n t) -> p n t", t=BLK)
        gate_all = spare[:, 0:2 * TOPK].rearrange("p (a k) t -> p a k t", k=TOPK)
        yT = spare[:, 2 * TOPK]
        o = spare[:, 2 * TOPK + 1].rearrange("p (t d) -> p t d", d=D)
        zs = sb("zs", [P, ZBUFS, TOPK, BLK])
        g = sb("g", [P, ZBUFS, TOPK, BLK])
        w2_split = w2_sb[:, SPLIT_CHUNKS.start:SPLIT_CHUNKS.stop:SPLIT_CHUNKS.step, :]
        s = tab_room[:, 0:SBUFS * BLK].rearrange("p (n t) -> p n t", n=SBUFS)
        s_hi = sb("s_hi", [P, SPLIT_BUFS, BLK], F32R)
        s_lo = sb("s_lo", [P, SPLIT_BUFS, BLK], F32R)

        z = [ctx.enter_context(nc.psum_tensor(f"z{i}", [P, BLK], F32)) for i in range(ZBUFS)]
        acc = [ctx.enter_context(nc.psum_tensor(f"acc{i}", [P, BLK], F32)) for i in range(2)]
        even = ctx.enter_context(nc.psum_tensor("even", [P, BLK], F32))
        odd = ctx.enter_context(nc.psum_tensor("odd", [P, BLK], F32))

        wa_in, w1_in, w2_in, ident_in, const_in, small_in = (
            sem(n) for n in ("wa_in", "w1_in", "w2_in", "ident_in", "const_in", "small_in"))
        tab_stats_ok, tab_moments, tab_var_eps_ok, tab_rstd_ok, tab_normed, tab_xT_psum, tab_xT_ok = (
            sem(n) for n in ("tab_stats_ok", "tab_moments", "tab_var_eps_ok", "tab_rstd_ok", "tab_normed",
                             "tab_xT_psum", "tab_xT_ok"))
        pe_in = [sem("pe_in_0"), sem("pe_in_1")]
        tab_psum, tab_raw, tab_ok, tab_late_ok, tab_stored = (
            sem(n) for n in ("tab_psum", "tab_raw", "tab_ok", "tab_late_ok", "tab_stored"))
        w1_hi_ok, w1_lo_ok = sem("w1_hi_ok"), sem("w1_lo_ok")
        warmed = sem("warmed")
        cols_psum, cols_ok, b2_ok, b2_twice_ok, pool_consts = (
            sem(n) for n in ("cols_psum", "cols_ok", "b2_ok", "b2_twice_ok", "pool_consts"))
        first_ids_in, ids_in, ids_now_ok, rows_gathered = (
            sem(n) for n in ("first_ids_in", "ids_in", "ids_now_ok", "rows_gathered"))
        row_stats_ok, row_moments_ok, row_var_eps_ok, row_rstd_ok, row_normed, row_xT_psum, row_xT_ok, v_psum, v_ok = (
            sem(n) for n in ("row_stats_ok", "row_moments_ok", "row_var_eps_ok", "row_rstd_ok", "row_normed",
                             "row_xT_psum", "row_xT_ok", "v_psum", "v_ok"))
        stats_ok, moments_ok, var_eps_ok, rstd_ok, shift_ok, normed = (
            sem(n) for n in ("stats_ok", "moments_ok", "var_eps_ok", "rstd_ok", "shift_ok", "normed"))
        q_psum, q_ok, k_psum, k_ok = (sem(n) for n in ("q_psum", "q_ok", "k_psum", "k_ok"))
        scores, att_in_ok, att_abs_ok, att_den_ok, att_rden_ok, att_between, att_ok = (
            sem(n) for n in ("scores", "att_in_ok", "att_abs_ok", "att_den_ok", "att_rden_ok", "att_between", "att_ok"))
        attended, h_mid_ok = sem("attended"), sem("h_mid_ok")
        xT_psum, xT_ok, x_hi_ok, x_lo_ok = sem("xT_psum"), sem("xT_ok"), sem("x_hi_ok"), sem("x_lo_ok")
        logits, top_ok, top_rel_ok, top_exp_ok, top_sum_ok, top_rsum_ok, gate_ok = (
            sem(n) for n in ("logits", "top_ok", "top_rel_ok", "top_exp_ok", "top_sum_ok", "top_rsum_ok", "gate_ok"))
        first_gates_psum, first_gates_ok = sem("first_gates_psum"), sem("first_gates_ok")
        gate_out, gate_in = sem("gate_out"), sem("gate_in")
        z_ok, zs_ok, g_ok, s_ok = sem("z_ok"), sem("zs_ok"), sem("g_ok"), sem("s_ok")
        w2_hi_ok, w2_lo_ok, s_hi_ok, s_lo_ok = sem("w2_hi_ok"), sem("w2_lo_ok"), sem("s_hi_ok"), sem("s_lo_ok")
        mixed, yT_ok, y_psum, o_ok, stored = (sem(n) for n in ("mixed", "yT_ok", "y_psum", "o_ok", "stored"))

        def run_blocks(body_of):
            eng, body = body_of
            body(0, 0)
            body(1, 1)
            with eng.Fori(1, blocks // 2 - 1) as j:
                body(j * 2, 0)
                body(j * 2 + 1, 1)
            body(blocks - 2, 0, rows_left=False)
            body(blocks - 1, 1, rows_left=False, front_left=False)

        def first(b, n=1):
            return isinstance(b, int) and b < n


        def tab_bank(j):
            return (z[3], acc[0], acc[1])[j % TAB_BANKS]

        block = ctx.enter_context(nc.Block())

        @block.sync
        def _(sp):
            def spread_gate(a, par):
                sp.wait_ge(gate_ok, a + 1)
                sp.dma_start(gate_d[par].rearrange("k (t p) -> p k t", p=P), gate[:]).then_inc(gate_out, 16)
                sp.wait_ge(gate_out, a * 16)
                if not first(a, 2):
                    sp.wait_ge(zs_ok, a * CHUNKS - CHUNKS)
                sp.dma_start(gate_all[:, par], gate_d[par:par + 1].broadcast_to([P, TOPK, BLK])).then_inc(gate_in, 16)

            def store(b):
                sp.wait_ge(o_ok, b + 1)
                sp.dma_start(out_v[:, bass.ds(b * TILES, TILES), :], o).then_inc(stored, 16)

            pe_v, table_v = (x.rearrange("(p j) n -> p j n", j=tab_tiles) for x in (pe, table_d))
            sp.dma_start(ids[:, 0:TILES], tok_v[:, 0:TILES]).then_inc(first_ids_in, 16)
            for half in TAB_HALVES:
                sp.dma_start(tab[:, half, COLS_H], pe_v[:, half, :]).then_inc(pe_in[half.start > 0], 16)
            sp.dma_start(ident[:], ident_d).then_inc(ident_in, 16)
            sp.dma_start(wa[:, 0:3 * D], w_qkv).then_inc(wa_in, 16)
            sp.dma_start(wa[:, 3 * D:], w_gate).then_inc(wa_in, 16)
            sp.dma_start(b_all[:], b_qkv.rearrange("(o d) -> o d", o=1).broadcast_to([P, 3 * D])).then_inc(const_in, 16)
            sp.dma_start(small[ROW_B1:ROW_B2, :], b1.rearrange("e (c f) -> (e c) f", f=P)).then_inc(small_in, 16)
            sp.dma_start(small[ROW_B2:ROW_BQ, :], b2).then_inc(small_in, 16)
            sp.dma_start(small[ROW_BQ:ROWS, :], b_qkv[0:2 * D].rearrange("(r d) -> r d", d=D)).then_inc(small_in, 16)
            sp.dma_start(between[:], between_d).then_inc(const_in, 16)
            sp.dma_start(within[:], within_d).then_inc(const_in, 16)
            sp.wait_ge(rows_gathered, 16 * TILES)
            sp.dma_start(w1_raw[:].rearrange("p (e c) f -> p e (c f)", e=EXPERTS),
                         w1.rearrange("e d f -> d e f")).then_inc(w1_in, 16)
            sp.dma_start(w2_sb[:], w2.rearrange("e (c f) d -> f (e c) d", f=P)).then_inc(w2_in, 16)
            sp.dma_start(ids[:, TILES:], tok_v[:, TILES:]).then_inc(ids_in, 16)
            for j in range(0, tab_tiles, TAB_STORE):
                if j < TAB_EARLY:
                    sp.wait_ge(tab_ok, j // TAB_STORE + 1)
                else:
                    sp.wait_ge(tab_late_ok, j - TAB_EARLY + TAB_STORE)
                sp.dma_start(table_v[:, j:j + TAB_STORE, :], tab[:, j:j + TAB_STORE, :]).then_inc(tab_stored, 16)

            def body(b, par, rows_left=True, front_left=True):
                if not first(b):
                    store(b - 1)
                if front_left:
                    spread_gate(b + 1, 1 - par)

            run_blocks((sp, body))
            store(blocks - 1)
            sp.wait_ge(stored, 16 * blocks)

        @block.gpsimd
        def _(pool):
            def take_ids(a):
                if not first(a):
                    pool.wait_ge(rows_gathered, a * (16 * TILES))
                pool.tensor_copy(ids_now[:], ids[:, bass.ds(a * TILES, TILES)]).then_inc(ids_now_ok, 1)

            def await_ids(a):
                pool.wait_ge(ids_now_ok, a + 1)
                if not first(a, 2):
                    pool.wait_ge(h_mid_ok, a - 1)

            def gather(dst, table, t):
                pool.indirect_dma_start(out=dst, out_offset=None, in_=table,
                                        in_offset=bass.IndirectOffsetOnAxis(ap=ids_now[:, t:t + 1], axis=0)
                                        ).then_inc(rows_gathered, 16)

            def rstd_of(moments_ok, var_eps_ok, rstd_ok, a):
                pool.wait_ge(moments_ok, a * TILES + TILES)
                pool.tensor_tensor(var_eps[:], mean_var[:, :, 1], eps[:, 0:TILES], ALU.add).then_inc(var_eps_ok, 1)
                pool.wait_ge(var_eps_ok, a + 1)
                pool.tensor_tensor(rstd[:], var_eps[:], minus_half[:, 0:TILES], ALU.pow).then_inc(rstd_ok, 1)

            def exps(a):
                pool.wait_ge(top_rel_ok, a + 1)
                pool.tensor_tensor(top_exp[:], euler[:], top_rel[:], ALU.pow).then_inc(top_exp_ok, 1)

            def add(b, c):
                pool.wait_ge(g_ok, b * CHUNKS + (c + 1))
                if not (first(b) and c < SBUFS):
                    pool.wait_ge(mixed, b * CHUNKS + (c - SBUFS + 1))
                pool.tensor_tensor(s[:, c % SBUFS, :], g[:, c % ZBUFS, 0, :], g[:, c % ZBUFS, 1, :],
                                   ALU.add).then_inc(s_ok, 1)

            def add_bias(j):
                pair = tab[:, j:j + TAB_STORE, D:]
                pool.wait_ge(tab_raw, j + TAB_STORE)
                pool.tensor_tensor(pair, pair, b_all[0:tab_p, :].rearrange("p (o d) -> p o d", o=1).broadcast_to(
                    [tab_p, TAB_STORE, 3 * D]), ALU.add).then_inc(tab_ok, 1)

            pool.memset(minus_half[:], -0.5).then_inc(pool_consts, 1)
            pool.memset(eps[:], EPS).then_inc(pool_consts, 1)
            pool.memset(euler[:], float(np.e)).then_inc(pool_consts, 1)
            pool.wait_ge(pool_consts, 3)
            pool.wait_ge(first_ids_in, 16)
            take_ids(0)
            await_ids(0)
            for t in range(TILES):
                gather(rows[:, 0, t, COLS_H], pe, t)
            pool.wait_ge(tab_moments, tab_tiles)
            pool.tensor_tensor(tab_var_eps[:], tab_mean_var[:, :, 1], eps[0:tab_p, :], ALU.add).then_inc(tab_var_eps_ok, 1)
            pool.wait_ge(tab_var_eps_ok, 1)
            pool.tensor_tensor(tab_rstd[:], tab_var_eps[:], minus_half[0:tab_p, :], ALU.pow).then_inc(tab_rstd_ok, 1)
            rstd_of(row_moments_ok, row_var_eps_ok, row_rstd_ok, 0)
            pool.wait_ge(const_in, 48)
            add_bias(0)
            add_bias(2)
            rstd_of(moments_ok, var_eps_ok, rstd_ok, 0)
            exps(0)
            pool.wait_ge(ids_in, 16)
            take_ids(1)
            await_ids(1)
            pool.wait_ge(tab_stored, 16 * (tab_tiles // TAB_STORE))
            for t in range(TILES):
                gather(rows[:, 1, t, :], table_d, t)

            def body(b, par, rows_left=True, front_left=True):
                for c in range(CHUNKS):
                    if rows_left and c == POOL_AT["gather"][0]:
                        await_ids(b + 2)
                    add(b, c)
                    if rows_left and c == POOL_AT["ids"]:
                        take_ids(b + 2)
                    if rows_left and c in POOL_AT["gather"]:
                        t = POOL_AT["gather"].index(c)
                        gather(rows[:, par, t, :], table_d, t)
                    if front_left and c == POOL_AT["rstd"]:
                        rstd_of(moments_ok, var_eps_ok, rstd_ok, b + 1)
                    if front_left and c == POOL_AT["exp"]:
                        exps(b + 1)

            run_blocks((pool, body))

        @block.scalar
        def _(act):
            b1_col = cols[:, ROW_B1:ROW_B2]

            def round_off(dst, src, done):
                act.activation(dst, src, ACT.Copy).then_inc(done, 1)

            def copy(dst, bank, ready, count, done):
                act.wait_ge(ready, count)
                act.activation(dst, bank[:], ACT.Copy).then_inc(done, 1)

            def normalise(a, par):
                act.wait_ge(shift_ok, a + 1)
                for t in range(TILES):
                    act.activation(xn[:, t, :], h_mid[:, par, t, :], ACT.Identity, bias=minus_shift[:, t:t + 1],
                                   scale=rstd[:, t:t + 1]).then_inc(normed, 1)

            def x_high(a, par):
                act.wait_ge(xT_psum, a + 1)
                round_off(x_hi[:, par, :], even[:], x_hi_ok)
                act.activation(xT[:], even[:], ACT.Copy).then_inc(xT_ok, 1)

            def y_bias(b, par):
                act.wait_ge(mixed, b * CHUNKS + CHUNKS)
                if not first(b):
                    act.wait_ge(y_psum, b)
                act.activation(yT, acc[par][:], ACT.Identity, bias=b2_twice[:, 0:1]).then_inc(yT_ok, 1)

            def gelus(b, c):
                act.wait_ge(zs_ok, b * CHUNKS + (c + 1))
                if not (first(b) and c < ZBUFS):
                    act.wait_ge(s_ok, b * CHUNKS + (c - ZBUFS + 1))
                act.activation(g[:, c % ZBUFS], zs[:, c % ZBUFS], ACT.Gelu,
                               bias=b1_col[:, c:c + 1]).then_inc(g_ok, 1)

            def s_high(b, c):
                n = SPLIT_CHUNKS.index(c)
                if n >= SPLIT_BUFS:
                    act.wait_ge(mixed, b * CHUNKS + (SPLIT_CHUNKS[n - SPLIT_BUFS] + 1))
                elif not first(b):
                    act.wait_ge(mixed, (b - 1) * CHUNKS + (SPLIT_CHUNKS[-1] + 1))
                act.wait_ge(s_ok, b * CHUNKS + (c + 1))
                round_off(s_hi[:, n % SPLIT_BUFS, :], s[:, c % SBUFS, :], s_hi_ok)

            act.wait_ge(pool_consts, 3)
            act.activation(warm[:], eps[:, 0:TILES], ACT.Gelu).then_inc(warmed, 1)
            act.wait_ge(cols_psum, 1)
            act.activation(cols[:], even[:, 0:ROWS], ACT.Copy).then_inc(cols_ok, 1)

            def tab_turned(n):
                at = 4 * n
                tiles = min(4, tab_tiles - at)
                act.wait_ge(tab_xT_psum, n + 1)
                act.activation(tab_xnT[:, at:at + tiles, :],
                               z[n][:, 0:tiles * tab_p].rearrange("p (j r) -> p j r", j=tiles), ACT.Copy
                               ).then_inc(tab_xT_ok, 1)

            tab_turned(0)
            copy(xT[:], even, row_xT_psum, 1, row_xT_ok)
            act.wait_ge(q_psum, 1)
            act.activation(qT[:], odd[:], ACT.Identity, bias=cols[:, ROW_BQ:ROW_BQ + 1]).then_inc(q_ok, 1)
            tab_turned(1)
            tab_turned(2)

            def w1_high(experts):
                act.wait_ge(w1_in, 16)
                for e in experts:
                    part = slice(e * CHUNKS // EXPERTS, (e + 1) * CHUNKS // EXPERTS)
                    round_off(w1_hi[:, part], w1_raw[:, part], w1_hi_ok)

            def tab_rows(tiles):
                for j in tiles:
                    act.wait_ge(tab_psum, j + 1)
                    act.activation(tab[:, j, D:], tab_bank(j)[0:tab_p, 0:3 * D], ACT.Copy).then_inc(tab_raw, 1)

            w1_high(range(0, 4))
            tab_rows(range(0, TAB_EARLY))
            w1_high(range(4, EXPERTS))
            normalise(0, 0)
            x_high(0, 0)
            act.wait_ge(b2_twice_ok, 1)
            act.wait_ge(w2_in, 16)
            round_off(w2_hi[:], w2_split, w2_hi_ok)
            for k in range(TOPK):
                copy(gate_all[:, 0, k, :], acc[k], first_gates_psum, k + 1, first_gates_ok)

            def body(b, par, rows_left=True, front_left=True):
                for c in range(CHUNKS):
                    gelus(b, c)
                    if c - HI_LAG in SPLIT_CHUNKS:
                        s_high(b, c - HI_LAG)
                    elif CHUNKS + c - HI_LAG in SPLIT_CHUNKS and not first(b):
                        s_high(b - 1, CHUNKS + c - HI_LAG)
                    if c == ACT_AT["yT"] and not first(b):
                        y_bias(b - 1, 1 - par)
                    if front_left and c == ACT_AT["norm"]:
                        normalise(b + 1, 1 - par)
                    if front_left and c == ACT_AT["x_hi"]:
                        x_high(b + 1, 1 - par)
                    if front_left and c == ACT_AT["q"] + first(b):
                        copy(qT[:], even, q_psum, b + 2, q_ok)
                    if front_left and c == ACT_AT["k"] + first(b):
                        copy(kT[:], odd, k_psum, b + 2, k_ok)

            run_blocks((act, body))
            for c in range(CHUNKS - HI_LAG, CHUNKS):
                if c in SPLIT_CHUNKS:
                    s_high(blocks - 1, c)
            y_bias(blocks - 1, 1)

        @block.vector
        def _(dve):
            def bn_stats(src, done):
                for t in range(TILES):
                    dve.bn_stats(stats[:, t, :], src[:, t, :]).then_inc(done, 1)

            def statistics(a, par):
                dve.wait_ge(h_mid_ok, a + 1)
                bn_stats(h_mid[:, par], stats_ok)

            def await_statistics(a):
                dve.wait_ge(stats_ok, a * TILES + TILES)

            def moments(done):
                for t in range(TILES):
                    dve.bn_aggr(mean_var[:, t, :], stats[:, t, :]).then_inc(done, 1)

            def shift(a):
                dve.wait_ge(rstd_ok, a + 1)
                dve.scalar_tensor_tensor(out=minus_shift[:], in0=mean_var[:, :, 0], scalar=-1.0, in1=rstd[:],
                                         op0=ALU.mult, op1=ALU.mult).then_inc(shift_ok, 1)

            def low(dst, full, hi, hi_ok, count, done):
                dve.wait_ge(hi_ok, count)
                dve.tensor_tensor(dst, full, hi.bitcast(F32), ALU.subtract).then_inc(done, 1)

            def diagonal(n):
                at = (n % 2) * 2 * P
                return slice(at, at + P)

            def att_seq(a, r):
                bank = (even, odd)[r]
                dve.wait_ge(scores, a * SEQS + (r + 1))
                for n in (2 * r, 2 * r + 1):
                    dve.tensor_tensor_reduce(att_in[:, n, :], bank[:, diagonal(n)], within[:], 1.0, 0.0,
                                             ALU.mult, ALU.add, att_sum[:, n:n + 1]).then_inc(att_in_ok, 1)
                dve.tensor_tensor(att[:, r, :], bank[:, 0:SCORE_W], between[:], ALU.mult).then_inc(att_between, 1)

            def att_norm(a):
                dve.wait_ge(att_in_ok, a * TILES + TILES)
                dve.scalar_tensor_tensor(out=att_abs[:], in0=att_sum[:], scalar=-1.0, in1=att_sum[:],
                                         op0=ALU.mult, op1=ALU.max).then_inc(att_abs_ok, 1)
                dve.wait_ge(att_abs_ok, a + 1)
                dve.tensor_scalar(att_den[:], att_abs[:], 1.0, None, ALU.max).then_inc(att_den_ok, 1)
                dve.wait_ge(att_den_ok, a + 1)
                dve.reciprocal(att_rden[:], att_den[:]).then_inc(att_rden_ok, 1)
                dve.wait_ge(att_rden_ok, a + 1)
                for n in range(TILES):
                    here = att[:, n // 2, diagonal(n)]
                    dve.wait_ge(att_between, a * SEQS + (n // 2 + 1))
                    dve.scalar_tensor_tensor(out=here, in0=att_in[:, n, :], scalar=att_rden[:, n:n + 1], in1=here,
                                             op0=ALU.mult, op1=ALU.add).then_inc(att_ok, 1)

            def residual(a, par):
                dve.wait_ge(attended, a + 1)
                if not first(a, 2):
                    dve.wait_ge(o_ok, a - 1)
                dve.tensor_tensor(h_mid[:, par], odd[:].rearrange("p (t d) -> p t d", t=TILES), rows[:, par, :, COLS_H],
                                  ALU.add).then_inc(h_mid_ok, 1)

            def await_logits(a):
                dve.wait_ge(logits, a + 1)

            def top_two(a):
                for t in range(TILES):
                    dve.max(top[:, t, :], odd[:, t * EXPERTS:(t + 1) * EXPERTS]).then_inc(top_ok, 1)
                dve.wait_ge(top_ok, a * TILES + TILES)
                dve.tensor_tensor(top_rel[:], top[:, :, 0:TOPK], top[:, :, 0:1].broadcast_to([P, TILES, TOPK]),
                                  ALU.subtract).then_inc(top_rel_ok, 1)

            def gates(a):
                dve.wait_ge(top_exp_ok, a + 1)
                dve.tensor_tensor(top_sum[:], top_exp[:, :, 0], top_exp[:, :, 1], ALU.add).then_inc(top_sum_ok, 1)
                dve.wait_ge(top_sum_ok, a + 1)
                dve.reciprocal(top_rsum[:], top_sum[:]).then_inc(top_rsum_ok, 1)
                dve.wait_ge(top_rsum_ok, a + 1)
                if first(a, 2):
                    if not first(a):
                        dve.wait_ge(first_gates_ok, TOPK)
                else:
                    dve.wait_ge(gate_out, (a - 1) * 16)
                dve.tensor_tensor(gate[:], top_exp[:].rearrange("p t k -> p k t"),
                                  top_rsum[:].rearrange("p (o t) -> p o t", o=1).broadcast_to([P, TOPK, TILES]),
                                  ALU.mult).then_inc(gate_ok, 1)

            def finish(b, par):
                dve.wait_ge(y_psum, b + 1)
                if not first(b):
                    dve.wait_ge(stored, b * 16)
                dve.tensor_tensor(o, even[:].rearrange("p (t d) -> p t d", t=TILES), h_mid[:, par],
                                  ALU.add).then_inc(o_ok, 1)

            def s_low(b, c):
                n = SPLIT_CHUNKS.index(c)
                low(s_lo[:, n % SPLIT_BUFS, :], s[:, c % SBUFS, :], s_hi[:, n % SPLIT_BUFS, :], s_hi_ok,
                    b * len(SPLIT_CHUNKS) + (n + 1), s_lo_ok)

            def scale(b, par, c):
                if c == 0:
                    if first(b):
                        dve.wait_ge(first_gates_ok, TOPK)
                    else:
                        dve.wait_ge(gate_in, b * 16)
                dve.wait_ge(z_ok, b * CHUNKS + (c + 1))
                if not (first(b) and c < ZBUFS):
                    dve.wait_ge(g_ok, b * CHUNKS + (c - ZBUFS + 1))
                both = z[c % ZBUFS][:].rearrange("p (o n) -> p o n", o=1).broadcast_to([P, TOPK, BLK])
                dve.tensor_tensor(zs[:, c % ZBUFS], both, gate_all[:, par], ALU.mult).then_inc(zs_ok, 1)

            for n, half in enumerate(TAB_HALVES):
                dve.wait_ge(pe_in[n], 16)
                for j in range(half.start, half.stop):
                    dve.bn_stats(tab_stats[:, j, :], tab[:, j, COLS_H]).then_inc(tab_stats_ok, 1)
                dve.wait_ge(tab_stats_ok, half.stop)
                for j in range(half.start, half.stop):
                    dve.bn_aggr(tab_mean_var[:, j, :], tab_stats[:, j, :]).then_inc(tab_moments, 1)
            def tab_normalise(half):
                for j in range(half.start, half.stop):
                    dve.tensor_scalar(tab_xn[:, j, :], tab[:, j, COLS_H], tab_mean_var[:, j, 0:1],
                                      tab_rstd[:, j:j + 1], ALU.subtract, ALU.mult).then_inc(tab_normed, 1)

            dve.wait_ge(rows_gathered, 16 * TILES)
            bn_stats(rows[:, 0, :, COLS_H], row_stats_ok)
            dve.wait_ge(row_stats_ok, TILES)
            moments(row_moments_ok)
            dve.wait_ge(tab_rstd_ok, 1)
            tab_normalise(TAB_HALVES[0])
            dve.wait_ge(row_rstd_ok, 1)
            for t in range(TILES):
                dve.tensor_scalar(xn[:, t, :], rows[:, 0, t, COLS_H], mean_var[:, t, 0:1], rstd[:, t:t + 1],
                                  ALU.subtract, ALU.mult).then_inc(row_normed, 1)
            tab_normalise(TAB_HALVES[1])
            dve.wait_ge(cols_ok, 1)
            dve.reduce_sum(b2_sum[:], cols[:, ROW_B2:ROW_BQ], AX_X).then_inc(b2_ok, 1)
            dve.wait_ge(b2_ok, 1)
            dve.tensor_scalar(b2_twice[:], b2_sum[:], float(TOPK), None, ALU.mult).then_inc(b2_twice_ok, 1)

            def w1_low(experts):
                for e in experts:
                    part = slice(e * CHUNKS // EXPERTS, (e + 1) * CHUNKS // EXPERTS)
                    low(w1_lo[:, part], w1_raw[:, part], w1_hi[:, part], w1_hi_ok, e + 1, w1_lo_ok)

            def tab_late(tiles):
                for j in tiles:
                    dve.wait_ge(tab_psum, j + 1)
                    dve.tensor_tensor(tab[:, j, D:], tab_bank(j)[0:tab_p, 0:3 * D], b_all[0:tab_p, :], ALU.add
                                      ).then_inc(tab_late_ok, 1)

            dve.wait_ge(k_psum, 1)
            dve.tensor_scalar(kT[:], z[3][:], cols[:, ROW_BK:ROW_BK + 1], None, ALU.add).then_inc(k_ok, 1)
            dve.wait_ge(const_in, 48)
            dve.wait_ge(v_psum, 1)
            dve.tensor_tensor(rows[:, 0, :, COLS_V], acc[0][:].rearrange("p (t d) -> p t d", t=TILES),
                              b_all[:, 2 * D:].rearrange("p (o d) -> p o d", o=1).broadcast_to([P, TILES, D]),
                              ALU.add).then_inc(v_ok, 1)
            att_seq(0, 0)
            att_seq(0, 1)
            att_norm(0)
            w1_low(range(0, 4))
            residual(0, 0)
            statistics(0, 0)
            await_statistics(0)
            moments(moments_ok)
            tab_late(range(TAB_EARLY, TAB_EARLY + 2))
            shift(0)
            tab_late(range(TAB_EARLY + 2, tab_tiles))
            w1_low(range(4, 6))
            low(x_lo[:, 0], even[:], x_hi[:, 0], xT_ok, 1, x_lo_ok)
            w1_low(range(6, EXPERTS))
            await_logits(0)
            top_two(0)
            low(w2_lo[:], w2_split, w2_hi[:], w2_hi_ok, 1, w2_lo_ok)
            gates(0)

            def body(b, par, rows_left=True, front_left=True):
                a, nxt = b + 1, 1 - par
                for c in range(CHUNKS):
                    if front_left and c == DVE_AT["moments"]:
                        await_statistics(a)
                    if front_left and c == DVE_AT["top"]:
                        await_logits(a)
                    scale(b, par, c)
                    if c - LO_LAG in SPLIT_CHUNKS:
                        s_low(b, c - LO_LAG)
                    elif CHUNKS + c - LO_LAG in SPLIT_CHUNKS and not first(b):
                        s_low(b - 1, CHUNKS + c - LO_LAG)
                    if c == DVE_AT["out"] and not first(b):
                        finish(b - 1, nxt)
                    if front_left and c == DVE_AT["att0"]:
                        att_seq(a, 0)
                    if front_left and c == DVE_AT["att1"]:
                        att_seq(a, 1)
                    if front_left and c == DVE_AT["att2"]:
                        att_norm(a)
                    if front_left and c == DVE_AT["h_mid"]:
                        residual(a, nxt)
                    if front_left and c == DVE_AT["stats"]:
                        statistics(a, nxt)
                    if front_left and c == DVE_AT["moments"]:
                        moments(moments_ok)
                    if front_left and c == DVE_AT["shift"]:
                        shift(a)
                    if front_left and c == DVE_AT["x_lo"]:
                        low(x_lo[:, nxt], even[:], x_hi[:, nxt], xT_ok, a + 1, x_lo_ok)
                    if front_left and c == DVE_AT["top"]:
                        top_two(a)
                    if front_left and c == DVE_AT["gate"]:
                        gates(a)

            run_blocks((dve, body))
            for c in range(CHUNKS - LO_LAG, CHUNKS):
                if c in SPLIT_CHUNKS:
                    s_low(blocks - 1, c)
            finish(blocks - 1, 1)

        @block.tensor
        def _(te):
            def passes(psum, w_hi, w_lo, m_hi, m_lo, start=True, stop=True):
                te.matmul(psum, w_hi, m_hi, start=start, stop=False)
                te.matmul(psum, w_hi, m_lo, start=False, stop=False)
                return te.matmul(psum, w_lo, m_hi, start=False, stop=stop)

            def turn(bank, tile_of, done):
                for t in range(TILES):
                    tr = te.transpose(bank[:, t * P:(t + 1) * P], tile_of(t), ident[:])
                tr.then_inc(done, 1)

            def q_turn(a, par):
                te.wait_ge(rows_gathered, a * (16 * TILES) + 16 * TILES)
                if not first(a):
                    te.wait_ge(x_lo_ok, a)
                turn(even, lambda t: rows[:, par, t, COLS_Q], q_psum)

            def k_turn(a, par):
                if not first(a):
                    te.wait_ge(top_rel_ok, a)
                turn(odd, lambda t: rows[:, par, t, COLS_K], k_psum)

            def score(a, r):
                if r == 0:
                    te.wait_ge(q_ok, a + 1)
                te.wait_ge(k_ok, a + 1)
                bank, at = (even, odd)[r], r * SEQ
                te.matmul(bank[:, 0:2 * P], kT[:, at:at + P], qT[:, at:at + 2 * P], start=True, stop=True)
                te.matmul(bank[:, 2 * P:3 * P], kT[:, at + P:at + 2 * P], qT[:, at + P:at + 2 * P],
                          start=True, stop=True).then_inc(scores, 1)

            def y_turn(b, bank_read, count):
                te.wait_ge(bank_read, count)
                te.wait_ge(yT_ok, b + 1)
                turn(even, lambda t: yT[:, t * P:(t + 1) * P], y_psum)

            def attend(a, par):
                te.wait_ge(att_ok, a * TILES + TILES)
                for r in range(SEQS):
                    at, t0 = r * SEQ, 2 * r
                    v0, v1 = rows[:, par, t0, COLS_V], rows[:, par, t0 + 1, COLS_V]
                    te.matmul(odd[:, at:at + P], att[:, r, 0:P], v0, start=True, stop=True)
                    te.matmul(odd[:, at + P:at + 2 * P], att[:, r, P:2 * P], v0, start=True, stop=False)
                    mm = te.matmul(odd[:, at + P:at + 2 * P], att[:, r, 2 * P:3 * P], v1, start=False, stop=True)
                mm.then_inc(attended, 1)

            def x_turn(a):
                if not first(a, 2):
                    te.wait_ge(o_ok, a - 1)
                te.wait_ge(normed, a * TILES + TILES)
                turn(even, lambda t: xn[:, t, :], xT_psum)

            def logit(a):
                te.wait_ge(xT_ok, a + 1)
                te.wait_ge(h_mid_ok, a + 1)
                for t in range(TILES):
                    tok_t = slice(t * P, (t + 1) * P)
                    mm = te.matmul(odd[:, t * EXPERTS:(t + 1) * EXPERTS], xT[:, tok_t], wa[:, 3 * D:],
                                   start=True, stop=True)
                mm.then_inc(logits, 1)

            def spread_first_gates():
                te.wait_ge(gate_ok, 1)
                for k in range(TOPK):
                    for t in range(TILES):
                        mm = te.matmul(acc[k][:, t * P:(t + 1) * P], gate[:, k, t:t + 1].broadcast_to([P, P]), ident[:],
                                       start=True, stop=True)
                    mm.then_inc(first_gates_psum, 1)

            def hidden(b, par, c):
                if not (first(b) and c < ZBUFS):
                    te.wait_ge(zs_ok, b * CHUNKS + (c - ZBUFS + 1))
                passes(z[c % ZBUFS][:], w1_hi[:, c, :], w1_lo[:, c, :], x_hi[:, par], x_lo[:, par]).then_inc(z_ok, 1)

            def mix(b, par, c):
                if c in SPLIT_CHUNKS:
                    n = SPLIT_CHUNKS.index(c)
                    te.wait_ge(s_lo_ok, b * len(SPLIT_CHUNKS) + (n + 1))
                else:
                    te.wait_ge(s_ok, b * CHUNKS + (c + 1))
                if c == 0 and not first(b, 2):
                    te.wait_ge(yT_ok, b - 1)
                ends = dict(start=c == 0, stop=c == CHUNKS - 1)
                if c in SPLIT_CHUNKS:
                    mm = passes(acc[par][:], w2_hi[:, n, :], w2_lo[:, n, :], s_hi[:, n % SPLIT_BUFS, :],
                                s_lo[:, n % SPLIT_BUFS, :], **ends)
                else:
                    mm = te.matmul(acc[par][:], w2_sb[:, c, :], s[:, c % SBUFS, :], **ends)
                mm.then_inc(mixed, 1)

            def keep_warm(n):
                for _ in range(n):
                    te.matmul(acc[1][:, 0:P], ident[:], ident[:], start=True, stop=True)

            te.wait_ge(ident_in, 16)
            keep_warm(WARM_UPS)
            te.wait_ge(small_in, 48)
            te.transpose(even[:, 0:ROWS], small[:], ident[0:ROWS, 0:ROWS]).then_inc(cols_psum, 1)

            def tab_turn(n):
                at = 4 * n
                for j in range(at, min(at + 4, tab_tiles)):
                    te.wait_ge(tab_normed, j + 1)
                    tr = te.transpose(z[n][:, (j - at) * tab_p:(j - at + 1) * tab_p], tab_xn[:, j, :],
                                      ident[0:tab_p, 0:tab_p])
                tr.then_inc(tab_xT_psum, 1)

            def tab_rows(tiles):
                for j in tiles:
                    te.wait_ge(tab_xT_ok, j // 4 + 1)
                    if j >= TAB_BANKS:
                        before = j - TAB_BANKS
                        if before < TAB_EARLY:
                            te.wait_ge(tab_raw, before + 1)
                        else:
                            te.wait_ge(tab_late_ok, before - TAB_EARLY + 1)
                    bank = tab_bank(j)[0:tab_p, 0:3 * D]
                    te.matmul(bank, tab_xnT[:, j, :], wa[:, 0:3 * D], start=True, stop=True).then_inc(tab_psum, 1)

            tab_turn(0)
            te.wait_ge(row_normed, TILES)
            te.wait_ge(cols_ok, 1)
            turn(even, lambda t: xn[:, t, :], row_xT_psum)
            keep_warm(WARM_UPS_AGAIN)
            te.wait_ge(wa_in, 32)
            te.wait_ge(row_xT_ok, 1)
            te.matmul(odd[:], wa[:, 0:D], xT[:], start=True, stop=True).then_inc(q_psum, 1)
            te.matmul(z[3][:], wa[:, D:2 * D], xT[:], start=True, stop=True).then_inc(k_psum, 1)
            for t in range(TILES):
                at = slice(t * P, (t + 1) * P)
                mm = te.matmul(acc[0][:, at], xT[:, at], wa[:, 2 * D:3 * D], start=True, stop=True)
            mm.then_inc(v_psum, 1)
            score(0, 0)
            score(0, 1)
            tab_turn(1)
            tab_turn(2)
            te.wait_ge(v_ok, 1)
            tab_rows(range(0, 4))
            attend(0, 0)
            tab_rows(range(4, tab_tiles))
            x_turn(0)
            logit(0)
            te.wait_ge(w1_lo_ok, EXPERTS)

            def body(b, par, rows_left=True, front_left=True):
                a, nxt = b + 1, 1 - par
                for c in range(CHUNKS):
                    if c == 0:
                        te.wait_ge(x_lo_ok, b + 1)
                    hidden(b, par, c)
                    if c >= LAG:
                        if c == LAG and first(b):
                            te.wait_ge(w2_lo_ok, 1)
                        mix(b, par, c - LAG)
                    elif not first(b):
                        mix(b - 1, nxt, CHUNKS + c - LAG)
                    if first(b) and c == 1:
                        spread_first_gates()
                    if c == PE_AT["yT"] and not first(b):
                        if front_left:
                            y_turn(b - 1, att_between, a * SEQS + 1)
                        else:
                            y_turn(b - 1, x_lo_ok, b + 1)
                    if front_left and c == PE_AT["q"] + first(b):
                        q_turn(a, nxt)
                    if front_left and c == PE_AT["k"] + first(b):
                        k_turn(a, nxt)
                    if front_left and c == PE_AT["scores0"]:
                        score(a, 0)
                    if front_left and c == PE_AT["scores1"]:
                        score(a, 1)
                    if front_left and c == PE_AT["attended"]:
                        attend(a, nxt)
                    if front_left and c == PE_AT["xT"]:
                        x_turn(a)
                    if front_left and c == PE_AT["logits"]:
                        logit(a)

            run_blocks((te, body))
            for c in range(CHUNKS - LAG, CHUNKS):
                mix(blocks - 1, 1, c)
            y_turn(blocks - 1, o_ok, blocks - 1)


_INS = ["x", "L0_tok_pe", "L0_attn_W", "L0_attn_b", "L0_ffn_Wg", "L0_ffn_W1", "L0_ffn_b1", "L0_ffn_W2", "L0_ffn_b2"]


def kernel(**inputs):
    import concourse.bacc as bacc
    from concourse.bass_utils import run_bass_kernel_spmd

    nc = bacc.Bacc("TRN2", target_bir_lowering=False, num_devices=1)
    arrays = {f"in_{n}": np.ascontiguousarray(inputs[n]) for n in _INS}
    between, within = attention_factors()
    arrays.update(const_between=between, const_within=within, const_ident=np.eye(P, dtype=np.float32))
    args = [nc.dram_tensor(n, a.shape, mybir.dt.from_np(a.dtype), kind="ExternalInput").ap() for n, a in arrays.items()]
    shape = (*inputs["x"].shape, D)
    out = nc.dram_tensor("out_h", shape, F32, kind="ExternalOutput").ap()
    table_d = nc.dram_tensor("row_q_k_v_by_id", (inputs["L0_tok_pe"].shape[0], TAB_W), F32, kind="Internal").ap()
    gate_d = nc.dram_tensor("gate_by_token", (2, TOPK, BLK), F32, kind="Internal").ap()
    build(nc, *args, out, table_d, gate_d)
    r = run_bass_kernel_spmd(nc, [arrays], core_ids=[0])
    return r.results[0]["out_h"]
```
